# Optimizing a Trainium2 kernel written in Bass

```python
import numpy as np
import jax
import jax.numpy as jnp

def _softmax(x, axis=-1):
    return jax.nn.softmax(x, axis=axis)

def _gelu(x):
    return jax.nn.gelu(x, approximate=True)

def _silu(x):
    return jax.nn.silu(x)

def _sigmoid(x):
    return jax.nn.sigmoid(x)

def _layernorm(x, axis=-1, eps=1e-05):
    m = jnp.mean(x, axis=axis, keepdims=True)
    v = jnp.var(x, axis=axis, keepdims=True)
    return (x - m) / jnp.sqrt(v + eps)

def _scatter_add(tgt, idx, src, axis=0):
    return tgt.at[idx].add(src)

def _segment_sum(src, seg, n):
    return jax.ops.segment_sum(src, seg, n)
kernel_name = 'mk_adj_resnorm_d1_adj_r2_2387cf'

def setup_inputs(seed: int=0):
    np.random.seed(seed)
    _w = jnp.asarray

    def _rec_inputs():
        import jax
        import jax.numpy as jnp
        _gk = jax.random.key(seed)
        x = -4.645e-05 + 0.05002 * jax.random.normal(jax.random.fold_in(_gk, 1), (8192, 128), jnp.float32)
        _w = (1.0 + jnp.arange(8192, dtype=jnp.float32)) ** (-0.5)
        _w = _w / _w.mean()
        _pij = jnp.clip(0.000976562 * _w[:, None] * _w[None, :], 0.0, 1.0)
        _a = jax.random.uniform(jax.random.fold_in(_gk, 2), (8192, 8192)) < _pij
        _af = _a.astype(jnp.float32)
        _af = _af / jnp.maximum(_af.sum(-1, keepdims=True), 1.0)
        adj = _af
        return (x, adj)
    x, adj = _rec_inputs()

    def _L0_gnn_setup():
        import jax, jax.numpy as jnp
        import numpy as np
        EPS = 1e-07
        MAX_TANH = 1.0 - 1e-06

        def _norm(v):
            return jnp.maximum(jnp.linalg.norm(v, axis=-1, keepdims=True), EPS)

        def log_map_zero(y):
            n = _norm(y)
            return jnp.arctanh(jnp.clip(n, 0.0, MAX_TANH)) * y / n

        def exp_map_zero(v):
            n = _norm(v)
            return jnp.tanh(n) * v / n

        def h_add(x, y):
            xy = jnp.sum(x * y, axis=-1, keepdims=True)
            x2 = jnp.sum(x * x, axis=-1, keepdims=True)
            y2 = jnp.sum(y * y, axis=-1, keepdims=True)
            num = (1.0 + 2.0 * xy + y2) * x + (1.0 - x2) * y
            den = 1.0 + 2.0 * xy + x2 * y2
            return num / jnp.maximum(den, EPS)

        def h_mul(x, W):
            return exp_map_zero(log_map_zero(x) @ W)
        key = jax.random.key(seed)
        k1, k2, k3, k4 = jax.random.split(key, 4)
        N, F_IN, F_OUT = (4096, 128, 128)
        x = 0.05 * jax.random.normal(k1, (N, F_IN), dtype=jnp.float32)
        a = (jax.random.uniform(k2, (N, N)) < 0.01).astype(jnp.float32)
        adj = a / jnp.maximum(a.sum(axis=1, keepdims=True), 1.0)
        lim_e = np.sqrt(6.0 / (F_IN + F_IN)) * np.sqrt(2.0)
        lim_l = np.sqrt(6.0 / (2 * F_IN + F_OUT)) * np.sqrt(2.0)
        embed = jax.random.uniform(k3, (F_IN, F_IN), minval=-lim_e, maxval=lim_e, dtype=jnp.float32)
        layer = jax.random.uniform(k4, (2 * F_IN, F_OUT), minval=-lim_l, maxval=lim_l, dtype=jnp.float32)
        embed_bias = jnp.zeros((F_IN,), dtype=jnp.float32)
        layer_bias = jnp.zeros((F_OUT,), dtype=jnp.float32)
        return {'x': x, 'adj': adj, 'embed': embed, 'layer': layer, 'embed_bias': embed_bias, 'layer_bias': layer_bias}
    _L0_gnn_all = _L0_gnn_setup()
    _L0_gnn_in = {k: v for k, v in _L0_gnn_all.items() if k in ('embed', 'layer', 'embed_bias', 'layer_bias')}
    del _L0_gnn_all
    return {'x': x, 'adj': adj, 'L0_gnn_embed': _L0_gnn_in['embed'], 'L0_gnn_layer': _L0_gnn_in['layer'], 'L0_gnn_embed_bias': _L0_gnn_in['embed_bias'], 'L0_gnn_layer_bias': _L0_gnn_in['layer_bias']}

def reference(x, adj, L0_gnn_embed, L0_gnn_layer, L0_gnn_embed_bias, L0_gnn_layer_bias):
    import jax
    import jax.numpy as jnp

    def _L0_gnn_ref(x, adj, embed, layer, embed_bias, layer_bias):
        import jax, jax.numpy as jnp
        import numpy as np
        EPS = 1e-07
        MAX_TANH = 1.0 - 1e-06

        def _norm(v):
            return jnp.maximum(jnp.linalg.norm(v, axis=-1, keepdims=True), EPS)

        def log_map_zero(y):
            n = _norm(y)
            return jnp.arctanh(jnp.clip(n, 0.0, MAX_TANH)) * y / n

        def exp_map_zero(v):
            n = _norm(v)
            return jnp.tanh(n) * v / n

        def h_add(x, y):
            xy = jnp.sum(x * y, axis=-1, keepdims=True)
            x2 = jnp.sum(x * x, axis=-1, keepdims=True)
            y2 = jnp.sum(y * y, axis=-1, keepdims=True)
            num = (1.0 + 2.0 * xy + y2) * x + (1.0 - x2) * y
            den = 1.0 + 2.0 * xy + x2 * y2
            return num / jnp.maximum(den, EPS)

        def h_mul(x, W):
            return exp_map_zero(log_map_zero(x) @ W)
        h = h_mul(x, embed)
        h = h_add(h, embed_bias[None, :])
        neigh = exp_map_zero(adj @ log_map_zero(h))
        out = h_mul(jnp.concatenate((x, neigh), axis=1), layer)
        out = h_add(out, layer_bias[None, :])
        return out
    x = _layernorm(x + _L0_gnn_ref(x, adj, L0_gnn_embed, L0_gnn_layer, L0_gnn_embed_bias, L0_gnn_layer_bias), axis=-1)
    return x

_drawn_inputs = setup_inputs


def setup_inputs(seed=0):
    import zlib

    import numpy as np

    out = dict(_drawn_inputs(seed))
    spreads = {'L0_gnn_embed_bias': (0.0, 0.1), 'L0_gnn_layer_bias': (0.0, 0.1)}
    factors = {}
    for name, (base, spread) in spreads.items():
        noise = np.random.default_rng([zlib.crc32(name.encode()), seed]).standard_normal(out[name].shape)
        drawn = base * np.exp(spread * noise) if base else spread * noise
        out[name] = jnp.asarray(drawn.astype(out[name].dtype))
    for name, factor in factors.items():
        out[name] = (out[name] * factor).astype(out[name].dtype)
    return out
```

```python
from contextlib import ExitStack

import concourse.bass as bass
from concourse import mybir

F32 = mybir.dt.float32
F32R = mybir.dt.float32r
ACT = mybir.ActivationFunctionType
ALU = mybir.AluOpType

P = 128
QUADS = 4
R = P // QUADS
EPS = 1e-7
MAX_TANH = 1.0 - 1e-6
LN_EPS = 1e-5

ROWS = 512
GROUPS = ROWS // R
STEP_COLS = 256
UNIT_TILES = 4
UNIT_COLS = UNIT_TILES * R
PERIOD = 16
STEPS = PERIOD // 2
KINDS = "SSMSSSMDSSMSSSMD"
SPLIT = [w for w in range(PERIOD) if KINDS[w] != "M"]
ORDER = {w: n for n, w in enumerate(SPLIT)}
OF_KIND = {w: [i for i in range(PERIOD) if KINDS[i] == KINDS[w]].index(w) for w in range(PERIOD)}
SLOT_OF_STEP = (0, 1, 2, 3, 4, 0, 5, 6, 3, 1, 0, 2, 4, 3, 5, 6)
IN_SLOTS = 7
STEPS_OF_SLOT = [[s for s in range(2 * STEPS) if SLOT_OF_STEP[s] == slot] for slot in range(IN_SLOTS)]
HALVES = 2
HALF = UNIT_TILES // HALVES
HALF_COLS = HALF * R
H_SLOTS = 4
LOW_BEHIND = 3
TILES = 8
ALL_TILES = PERIOD * UNIT_TILES
X_PARTS = 4
X_SLOTS = (IN_SLOTS - 2, IN_SLOTS)
DMA = 16

FRONT_PE = dict(turn_0=21, project_0=24, turn_1=23, project_1=25, even=27)
FRONT_ACT = dict(load_x=19, copy_0=21, copy_1=26, copy_products=28, even=19)
BACK_PE = dict(odd=2)
BACK_ACT = dict(odd=1, v_rooted=4, v_tanh=6, square_y=8, rooted=11, log=12, tanh=12, scale_bias=17, var_rooted=18,
                store=21)
BACK_DVE = dict(take_sums=7, norm_v=9, y_of_v=9, clamp=10, ask_log=15, ask_tanh=15, coefs=20, residual=20,
                variance=20, shift=22)
TURNED_EARLY = 5

PAIR_LINKS = 42
PAIR_ROOTS = 3


class Numbers:
    DOUBLE = ("sq", "clamped", "rsq", "norm", "tmp")
    SINGLE = ("lg", "zh", "arg", "rec", "alpha", "th", "dot", "c_y", "c_b", "beta", "m_norm")
    KINDS = 2 * len(DOUBLE) + len(SINGLE)

    def __init__(self, tensor, n):
        views = [tensor[:, n * i:n * (i + 2)] for i in range(0, 2 * len(self.DOUBLE), 2)]
        views += [tensor[:, n * i:n * (i + 1)] for i in range(2 * len(self.DOUBLE), self.KINDS)]
        (self.sq, self.clamped, self.rsq, self.norm, self.tmp, self.lg, self.zh, self.arg, self.rec, self.alpha,
         self.th, self.dot, self.c_y, self.c_b, self.beta, self.m_norm) = views
        self.n = n


def graph_layer(nc, x, adj, embed, layer, embed_bias, layer_bias, out):
    N, D = x.shape
    BLOCKS = adj.shape[0] // ROWS
    PAIRS = BLOCKS // 2
    assert D == P and N // QUADS // UNIT_COLS == PERIOD and STEP_COLS == 2 * UNIT_COLS and BLOCKS % 2 == 0
    assert len(SPLIT) * HALVES % H_SLOTS == 0 and H_SLOTS % HALVES == 0

    adj_v = adj.rearrange("(k g r) (q j c) -> k j q r g c", g=GROUPS, r=R, q=QUADS, c=STEP_COLS)
    x_part = x.rearrange("(q n t c) f -> n q c t f", q=QUADS, n=X_PARTS, c=R)
    x_pair = x.rearrange("(m j p t) f -> m p j t f", j=2, p=P, t=4)
    out_pair = out.rearrange("(m j p t) f -> m p j t f", j=2, p=P, t=4)

    with ExitStack() as ctx:
        def sb(name, shape, dt=F32):
            return ctx.enter_context(nc.sbuf_tensor(name, shape, dt))

        def sem(name):
            return ctx.enter_context(nc.semaphore(name))

        def over(name, shape, dt, offset):
            return nc.alloc_sbuf_tensor_at(name, shape, dt, offset=offset)

        def next_place():
            return (nc.sbuf_base + 31) // 32 * 32

        a_in, a_low = [], []
        for i in range(IN_SLOTS):
            if i == X_SLOTS[0]:
                x_all = over("x_all", [P, ALL_TILES, D], F32, next_place())
            a_low.append(over(f"a_low_{i}", [P, GROUPS, STEP_COLS], F32R, next_place()))
            a_in.append(sb(f"a_in_{i}", [P, GROUPS, STEP_COLS]))
        a_high = sb("a_high", [P, H_SLOTS, GROUPS, HALF_COLS], F32R)
        L_high = sb("L_high", [P, len(SPLIT) * UNIT_TILES, D], F32R)
        L_at = next_place()
        L_low = sb("L_low", [P, len(SPLIT) * UNIT_TILES, D], F32R)
        L_exact = over("L_exact", [P, len(SPLIT) * UNIT_TILES, D], F32, L_at)
        L_whole = sb("L_whole", [P, (PERIOD - len(SPLIT)) * UNIT_TILES, D])
        rows_at = next_place()
        x_rows = sb("x_rows", [P, TILES, D])
        y_rows = sb("y_rows", [P, TILES, D])
        side = sb("side", [P, TILES, D])
        lifted = sb("lifted", [P, 2, ROWS])
        lifted_sq = sb("lifted_sq", [P, 2, ROWS])
        embed_at = next_place()
        w_embed = sb("w_embed", [P, D + 1])
        b_embed = sb("b_embed", [P, D])
        w_x = sb("w_x", [P, D])
        w_v = sb("w_v", [P, D])
        b_layer = sb("b_layer", [P, D])
        ident = sb("ident", [P, P])
        ones = sb("ones", [P, 1])
        b_sq = sb("b_sq", [P, 2])
        layer_b = sb("layer_b", [P, 2])
        pair_numbers = Numbers(sb("pair_numbers", [P, Numbers.KINDS * TILES]), TILES)
        L_numbers = Numbers(over("L_numbers", [P, Numbers.KINDS * ALL_TILES], F32, rows_at), ALL_TILES)
        assert Numbers.KINDS * ALL_TILES <= 2 * TILES * D
        spare = over("spare", [P, 2, D], mybir.dt.bfloat16, embed_at)
        bias_at = embed_at + 4 * (D + 1) + 28
        sums = over("sums", [P, 4 * TILES], F32, bias_at)
        stats = over("stats", [P, TILES, 6], F32, bias_at + 4 * 4 * TILES)
        mean_sum = over("mean_sum", [P, TILES], F32, bias_at + 4 * 10 * TILES)

        psum = ctx.enter_context(nc.psum_tensor("psum", [P, 8, ROWS], F32))
        acc = [psum[:, j, :] for j in range(2)]
        ps_v = [psum[:, 2 + t // 4, P * (t % 4):P * (t % 4 + 1)] for t in range(TILES)]
        ps_x = [psum[:, 4 + t // 4, P * (t % 4):P * (t % 4 + 1)] for t in range(TILES)]
        ps_turn = psum[:, 6, :]
        ps_sum = psum[:, 7, :]
        ps_turn_L = [psum[:, j, :] for j in range(2)]
        ps_u = [psum[:, 2 + 2 * j:4 + 2 * j, 0:2 * (D + 1)].rearrange("p k (t c) -> p k t c", t=2) for j in range(2)]

        consts_in, ident_zero, consts_set, bias_done = (
            sem(n) for n in ("consts_in", "ident_zero", "consts_set", "bias_done"))
        x_in = [sem(f"x_in_{n}") for n in range(X_PARTS)]
        step_landed = [sem(f"step_landed_{i}") for i in range(IN_SLOTS)]
        unit_turned, high_made, half_multiplied = sem("unit_turned"), sem("high_made"), sem("half_multiplied")
        low_made = {"S": sem("low_made_pool"), "D": sem("low_made_dve")}
        block_copied, block_projected = sem("block_copied"), sem("block_projected")
        bias_rows_made, L_exact_made, L_high_made, L_low_made = (
            sem(n) for n in ("bias_rows_made", "L_exact_made", "L_high_made", "L_low_made"))
        COMMON = ("x_turned", "xT_made", "projected", "sq_clamped", "sq_rooted", "log_asked", "log_taken",
                  "tanh_asked", "tanh_taken", "coefs_made", "dve_step", "act_step")
        L_s = {n: sem(f"L_{n}") for n in COMMON + (
            "x_squared", "u_taken", "h_clamped", "h_rooted", "h_log_asked", "h_log_taken", "scale_made")}
        pair_s = {n: sem(f"pair_{n}") for n in COMMON + (
            "x_landed", "products_copied", "sums_taken", "v_clamped", "v_rooted", "v_normed", "v_tanh", "y_made",
            "squared", "bias_scaled", "res_made", "var_clamped", "var_rooted", "shift_made", "out_made", "stored")}

        block = ctx.enter_context(nc.Block())

        def wait(eng, s, value):
            if not isinstance(value, int) or value > 0:
                eng.wait_ge(s, value)

        def after_split(w, back, b, e):
            behind = 1 if ORDER[w] < back else 0
            return HALVES * (PERIOD * (b - behind) + SPLIT[ORDER[w] - back + behind * len(SPLIT)]) + e + 1

        def place(j, w):
            return SLOT_OF_STEP[STEPS * j + w // 2], UNIT_COLS * (w % 2)

        def halves_of(w):
            at = UNIT_COLS * (w % 2)
            for e in range(HALVES):
                n = HALVES * ORDER[w] + e
                yield e, n, slice(at + HALF_COLS * e, at + HALF_COLS * (e + 1)), n % H_SLOTS

        def L_tiles(w):
            if KINDS[w] == "M":
                return L_whole[:, UNIT_TILES * OF_KIND[w]:UNIT_TILES * (OF_KIND[w] + 1), :]
            return L_exact[:, UNIT_TILES * ORDER[w]:UNIT_TILES * (ORDER[w] + 1), :]

        def L_slots(w):
            return slice(UNIT_TILES * ORDER[w], UNIT_TILES * (ORDER[w] + 1))

        def steps_of(eng, s, base):
            done = [0]

            def step(ins):
                ins.then_inc(s, 1)
                done[0] += 1
                eng.wait_ge(s, base + done[0])
            step.done = done
            return step

        def run(hooks, w):
            for at, action in hooks:
                if at == w:
                    action()

        def hooks_of(slots, actions):
            return [(slots[name], action) for name, action in actions]

        def schedule(engine, blocks, front, back, L_hooks=(), finish=None):
            blocks(0, list(L_hooks) + front(0))
            blocks(1, back(0) + front(1))
            with engine.Fori(2, PAIRS) as m:
                blocks(m, back(m - 1) + front(m))
            if finish:
                finish()
            for _, action in back(PAIRS - 1):
                action()

        def nothing(f):
            return []

        @block.sync
        def _(sp):
            for n in range(X_PARTS):
                tiles = slice(ALL_TILES // X_PARTS * n, ALL_TILES // X_PARTS * (n + 1))
                for q in range(QUADS):
                    sp.dma_start(x_all[R * q:R * (q + 1), tiles, :], x_part[n, q]).then_inc(x_in[n], DMA)
            sp.wait_ge(x_in[X_PARTS - 2], QUADS * DMA)

            def blocks(m, hooks):
                for s in range(2 * STEPS):
                    slot = SLOT_OF_STEP[s]
                    n = STEPS_OF_SLOT[slot].index(s)
                    last = STEPS_OF_SLOT[slot][n - 1] - (2 * STEPS if n == 0 else 0)
                    wait(sp, half_multiplied, HALVES * (2 * PERIOD * m + 2 * last + 2))
                    if isinstance(m, int) and m == 0 and n == 0 and slot in range(*X_SLOTS):
                        sp.wait_ge(L_s["x_turned"], PERIOD)
                        sp.wait_ge(L_s["x_squared"], PERIOD)
                    for q in range(QUADS):
                        sp.dma_start(a_in[slot][R * q:R * (q + 1)], adj_v[2 * m + s // STEPS, s % STEPS, q])\
                            .then_inc(step_landed[slot], DMA)

            schedule(nc.sync, blocks, nothing, nothing)

        @block.vector
        def _(dve):
            v = nc.vector

            def turn(m, j, w):
                slot, at = place(j, w)
                users = STEPS_OF_SLOT[slot]
                uses = len(users) * m + users.index(STEPS * j + w // 2) + 1
                dve.wait_ge(step_landed[slot], QUADS * DMA * uses)
                unit = a_in[slot][:, :, at:at + UNIT_COLS]
                v.transpose(unit, unit).then_inc(unit_turned, 1)

            def low(m, j, w):
                slot = place(j, w)[0]
                for _, n, cols, high in halves_of(w):
                    dve.wait_ge(high_made, HALVES * len(SPLIT) * (2 * m + j) + n + 1)
                    v.tensor_tensor(a_low[slot][:, :, cols], a_in[slot][:, :, cols], a_high[:, high].bitcast(F32),
                                    ALU.subtract).then_inc(low_made["D"], 1)

            def blocks(m, hooks):
                for j in range(2):
                    for w in range(PERIOD):
                        at_start = isinstance(m, int) and m == 0 and j == 0
                        if not (at_start and w < TURNED_EARLY):
                            turn(m, j, w)
                        behind = (w - LOW_BEHIND) % PERIOD
                        if KINDS[behind] == "D" and w >= LOW_BEHIND:
                            low(m, j, behind)
                        elif KINDS[behind] == "D" and not at_start:
                            low(m if j else m - 1, 1 - j, behind)
                        run(hooks, PERIOD * j + w)

            def last_lows():
                for w in range(PERIOD - LOW_BEHIND, PERIOD):
                    if KINDS[w] == "D":
                        low(PAIRS - 1, 1, w)

            def root(N, step, n):
                tmp, rsq, clamped = N.tmp[:, 0:n], N.rsq[:, 0:n], N.clamped[:, 0:n]
                step(v.tensor_tensor(tmp, rsq, rsq, ALU.mult))
                step(v.tensor_tensor(tmp, tmp, clamped, ALU.mult))
                step(v.tensor_scalar(tmp, tmp, -0.5, 1.5, ALU.mult, ALU.add))
                step(v.tensor_tensor(rsq, rsq, tmp, ALU.mult))
                return v.tensor_tensor(N.norm[:, 0:n], clamped, rsq, ALU.mult)

            def log_argument(N, step):
                step(v.tensor_scalar(N.zh, N.norm[:, 0:N.n], MAX_TANH, None, ALU.min))
                step(v.tensor_scalar(N.arg, N.zh, -1.0, 1.0, ALU.mult, ALU.add))
                step(v.reciprocal(N.rec, N.arg))
                step(v.tensor_tensor(N.zh, N.zh, N.rec, ALU.mult))
                return v.tensor_scalar(N.arg, N.zh, 2.0, 1.0, ALU.mult, ALU.add)

            def artanh_over_norm(N, step):
                step(v.tensor_scalar(N.arg, N.arg, 1.0, None, ALU.subtract))
                step(v.reciprocal(N.rec, N.arg))
                step(v.tensor_tensor(N.zh, N.zh, N.lg, ALU.mult))
                step(v.tensor_tensor(N.zh, N.zh, N.rec, ALU.mult))
                return v.tensor_tensor(N.alpha, N.zh, N.rsq[:, 0:N.n], ALU.mult)

            def ask_log(N, step, s, count):
                dve.wait_ge(s["sq_rooted"], count + 1)
                step(root(N, step, 2 * N.n))
                log_argument(N, step).then_inc(s["log_asked"], 1)
                dve.wait_ge(s["log_asked"], count + 1)

            def ask_tanh(N, step, s, count):
                dve.wait_ge(s["log_taken"], count + 1)
                step(artanh_over_norm(N, step))
                step(v.tensor_tensor(N.m_norm, N.alpha, N.norm[:, N.n:2 * N.n], ALU.mult))
                v.tensor_scalar(N.m_norm, N.m_norm, EPS, None, ALU.max).then_inc(s["tanh_asked"], 1)
                dve.wait_ge(s["tanh_asked"], count + 1)

            def coefs(N, step, s, count, bb):
                x2, y_sq = N.tmp[:, 0:N.n], N.sq[:, N.n:2 * N.n]
                double = N.tmp[:, N.n:2 * N.n]
                dve.wait_ge(s["tanh_taken"], count + 1)
                step(v.reciprocal(N.rec, N.m_norm))
                step(v.tensor_tensor(N.beta, N.th, N.rec, ALU.mult))
                step(v.tensor_tensor(N.beta, N.beta, N.alpha, ALU.mult))
                v.tensor_tensor(double, N.dot, N.beta, ALU.mult)
                step(v.tensor_tensor(x2, N.beta, N.beta, ALU.mult))
                v.tensor_scalar(double, double, 2.0, 1.0, ALU.mult, ALU.add)
                step(v.tensor_tensor(x2, x2, y_sq, ALU.mult))
                step(v.scalar_tensor_tensor(out=N.c_b, in0=x2, scalar=bb, in1=double, op0=ALU.mult, op1=ALU.add))
                step(v.tensor_scalar(N.c_b, N.c_b, EPS, None, ALU.max))
                step(v.reciprocal(N.rec, N.c_b))
                v.scalar_tensor_tensor(out=N.c_y, in0=double, scalar=bb, in1=N.beta, op0=ALU.add, op1=ALU.mult)
                step(v.tensor_scalar(x2, x2, -1.0, 1.0, ALU.mult, ALU.add))
                v.tensor_tensor(N.c_y, N.c_y, N.rec, ALU.mult)
                v.tensor_tensor(N.c_b, x2, N.rec, ALU.mult).then_inc(s["coefs_made"], 1)
                dve.wait_ge(s["coefs_made"], count + 1)

            def make_numbers():
                N, s = L_numbers, L_s
                n = N.n
                step = steps_of(dve, s["dve_step"], 0)
                for g in range(PERIOD):
                    dve.wait_ge(s["projected"], g + 1)
                    u_rows = L_tiles(g).rearrange("p (k t) f -> p k t f", k=2)
                    dots = N.dot[:, UNIT_TILES * g:UNIT_TILES * (g + 1)].rearrange("p (k t) -> p k t", k=2)
                    v.tensor_copy(dots, ps_u[g % 2][:, :, :, D])
                    v.tensor_copy(u_rows, ps_u[g % 2][:, :, :, 0:D]).then_inc(s["u_taken"], 1)
                    dve.wait_ge(s["u_taken"], g + 1)
                    for i in range(UNIT_TILES):
                        u, t = L_tiles(g)[:, i, :], UNIT_TILES * g + i
                        last = v.tensor_tensor_reduce(out=side[:, t % TILES, :], in0=u, in1=u, scale=1.0, scalar=0.0,
                                                      op0=ALU.mult, op1=ALU.add, accum_out=N.sq[:, n + t:n + t + 1])
                step(last)
                early = iter(range(TURNED_EARLY))
                dve.wait_ge(s["x_squared"], PERIOD)
                v.tensor_scalar(N.clamped, N.sq, EPS * EPS, None, ALU.max).then_inc(s["sq_clamped"], 1)
                turn(0, 0, next(early))
                ask_log(N, step, s, 0)
                turn(0, 0, next(early))
                ask_tanh(N, step, s, 0)
                turn(0, 0, next(early))
                coefs(N, step, s, 0, b_sq[:, 0:1])
                h_sq, rest = N.clamped[:, 0:n], N.clamped[:, n:2 * n]
                v.tensor_tensor(h_sq, N.c_y, N.sq[:, n:2 * n], ALU.mult)
                step(v.tensor_tensor(rest, N.c_b, N.dot, ALU.mult))
                step(v.scalar_tensor_tensor(out=h_sq, in0=rest, scalar=2.0, in1=h_sq, op0=ALU.mult, op1=ALU.add))
                v.tensor_tensor(h_sq, h_sq, N.c_y, ALU.mult)
                step(v.tensor_tensor(rest, N.c_b, N.c_b, ALU.mult))
                step(v.scalar_tensor_tensor(out=h_sq, in0=rest, scalar=b_sq[:, 0:1], in1=h_sq,
                                            op0=ALU.mult, op1=ALU.add))
                v.tensor_scalar(h_sq, h_sq, EPS * EPS, None, ALU.max).then_inc(s["h_clamped"], 1)
                turn(0, 0, next(early))
                dve.wait_ge(s["h_rooted"], 1)
                step(root(N, step, n))
                log_argument(N, step).then_inc(s["h_log_asked"], 1)
                dve.wait_ge(s["h_log_asked"], 1)
                turn(0, 0, next(early))
                dve.wait_ge(s["h_log_taken"], 1)
                step(artanh_over_norm(N, step))
                v.tensor_tensor(N.c_b, N.c_b, N.alpha, ALU.mult)
                v.tensor_tensor(N.c_y, N.c_y, N.alpha, ALU.mult).then_inc(s["scale_made"], 1)
                dve.wait_ge(s["scale_made"], 1)
                for w in early:
                    turn(0, 0, w)

            def L_rows(w):
                dve.wait_ge(bias_rows_made, w + 1)
                for i in range(UNIT_TILES):
                    t, row = UNIT_TILES * w + i, L_tiles(w)[:, i, :]
                    last = v.scalar_tensor_tensor(out=row, in0=row, scalar=L_numbers.c_y[:, t:t + 1],
                                                  in1=side[:, t % TILES, :], op0=ALU.mult, op1=ALU.add)
                last.then_inc(L_exact_made, 1)

            def back(f):
                s, N, step = pair_s, pair_numbers, steps_of(dve, pair_s["dve_step"], f * PAIR_LINKS)
                n = TILES
                v_sq, v_dot, x_sq, x_dot = (sums[:, n * i:n * (i + 1)] for i in range(4))

                def take_sums():
                    dve.wait_ge(block_projected, 2 * f + 2)
                    v.tensor_copy(sums[:, :], ps_sum[:, 0:4 * n]).then_inc(s["sums_taken"], 1)
                    dve.wait_ge(s["sums_taken"], f + 1)
                    v.tensor_scalar(N.clamped[:, 0:n], v_sq, EPS * EPS, None, ALU.max).then_inc(s["v_clamped"], 1)

                def norm_v():
                    dve.wait_ge(s["v_rooted"], f + 1)
                    root(N, step, n).then_inc(s["v_normed"], 1)
                    dve.wait_ge(s["v_normed"], f + 1)

                def y_of_v():
                    x2, rest = N.tmp[:, 0:n], N.tmp[:, n:2 * n]
                    dve.wait_ge(s["v_tanh"], f + 1)
                    step(v.tensor_tensor(N.th, N.th, N.rsq[:, 0:n], ALU.mult))
                    dve.wait_ge(s["products_copied"], f + 1)
                    wait(dve, s["stored"], DMA * f)
                    for t in range(n):
                        last = v.scalar_tensor_tensor(out=y_rows[:, t, :], in0=ps_v[t], scalar=N.th[:, t:t + 1],
                                                      in1=side[:, t, :], op0=ALU.mult, op1=ALU.add)
                    last.then_inc(s["y_made"], 1)
                    v.tensor_tensor(rest, N.th, v_dot, ALU.mult)
                    step(v.tensor_tensor(x2, N.th, N.th, ALU.mult))
                    v.tensor_tensor(N.dot, x_dot, rest, ALU.add)
                    step(v.tensor_tensor(x2, x2, v_sq, ALU.mult))
                    step(v.tensor_tensor(N.sq[:, 0:n], x_sq, x2, ALU.add))

                def clamp():
                    dve.wait_ge(s["squared"], n * (f + 1))
                    v.tensor_scalar(N.clamped, N.sq, EPS * EPS, None, ALU.max).then_inc(s["sq_clamped"], 1)

                def residual():
                    dve.wait_ge(s["bias_scaled"], f + 1)
                    step(v.tensor_tensor(side[:, :, :], side[:, :, :], x_rows[:, :, :], ALU.add))
                    for t in range(n):
                        last = v.scalar_tensor_tensor(out=y_rows[:, t, :], in0=y_rows[:, t, :],
                                                      scalar=N.c_y[:, t:t + 1], in1=side[:, t, :],
                                                      op0=ALU.mult, op1=ALU.add)
                    last.then_inc(s["res_made"], 1)

                def variance():
                    dve.wait_ge(s["res_made"], f + 1)
                    for t in range(n):
                        last = v.bn_stats(stats[:, t, :], y_rows[:, t, :])
                    step(last)
                    mean_0, mean_1, cv_0, cv_1 = (stats[:, :, i] for i in (1, 4, 2, 5))
                    v.tensor_tensor(mean_sum[:, :], mean_0, mean_1, ALU.add)
                    v.tensor_tensor(N.zh, cv_0, cv_1, ALU.add)
                    step(v.tensor_tensor(N.arg, mean_0, mean_1, ALU.subtract))
                    step(v.tensor_tensor(N.arg, N.arg, N.arg, ALU.mult))
                    step(v.scalar_tensor_tensor(out=N.zh, in0=N.arg, scalar=D / 4.0, in1=N.zh,
                                                op0=ALU.mult, op1=ALU.add))
                    v.tensor_scalar(N.clamped[:, 0:n], N.zh, 1.0 / D, LN_EPS, ALU.mult, ALU.add)\
                        .then_inc(s["var_clamped"], 1)

                def shift():
                    dve.wait_ge(s["var_rooted"], f + 1)
                    step(root(N, step, n))
                    v.scalar_tensor_tensor(out=N.tmp[:, 0:n], in0=mean_sum[:, :], scalar=-0.5,
                                           in1=N.rsq[:, 0:n], op0=ALU.mult, op1=ALU.mult)\
                        .then_inc(s["shift_made"], 1)
                    assert step.done[0] == PAIR_LINKS, step.done

                return hooks_of(BACK_DVE, (
                    ("take_sums", take_sums), ("norm_v", norm_v), ("y_of_v", y_of_v), ("clamp", clamp),
                    ("ask_log", lambda: ask_log(N, step, s, f)), ("ask_tanh", lambda: ask_tanh(N, step, s, f)),
                    ("coefs", lambda: coefs(N, step, s, f, b_sq[:, 1:2])), ("residual", residual),
                    ("variance", variance), ("shift", shift)))

            v.memset(ones[:, :], 1.0).then_inc(consts_set, 1)
            dve.wait_ge(consts_in, 5 * DMA)
            for i, (a, b, total) in enumerate(((b_embed, b_embed, b_sq[:, 0:1]), (b_layer, b_layer, b_sq[:, 1:2]),
                                               (w_embed, b_embed, w_embed[:, D:D + 1]), (w_x, b_layer, layer_b[:, 0:1]),
                                               (w_v, b_layer, layer_b[:, 1:2]))):
                v.tensor_tensor_reduce(out=side[:, i, :], in0=a[:, 0:D], in1=b[:, :], scale=1.0, scalar=0.0,
                                       op0=ALU.mult, op1=ALU.add, accum_out=total).then_inc(bias_done, 1)
            dve.wait_ge(bias_done, 5)
            make_numbers()
            L_rows(0)
            schedule(nc.vector, blocks, nothing, back, [(w - 1, lambda w=w: L_rows(w)) for w in range(1, PERIOD)],
                     last_lows)

        @block.scalar
        def _(act):
            a = nc.scalar

            def blocks(m, hooks):
                for j in range(2):
                    b = 2 * m + j
                    for w in range(PERIOD):
                        if KINDS[w] != "M":
                            act.wait_ge(unit_turned, PERIOD * b + w + 1)
                            for e, _, cols, high in halves_of(w):
                                wait(act, half_multiplied, after_split(w, H_SLOTS // HALVES, b, e))
                                a.activation(a_high[:, high], a_in[place(j, w)[0]][:, :, cols], ACT.Copy)\
                                    .then_inc(high_made, 1)
                        run(hooks, PERIOD * j + w)

            def estimate_root(N, s, name, base, n):
                step = steps_of(act, s["act_step"], base)
                step(a.activation(N.rsq[:, 0:n], N.clamped[:, 0:n], ACT.Ln))
                a.activation(N.rsq[:, 0:n], N.rsq[:, 0:n], ACT.Exp, scale=-0.5).then_inc(s[name], 1)

            def take_log(N, s, asked, taken, count):
                act.wait_ge(s[asked], count + 1)
                a.activation(N.lg, N.arg, ACT.Ln).then_inc(s[taken], 1)

            def take_tanh(N, s, count):
                act.wait_ge(s["tanh_asked"], count + 1)
                a.activation(N.th, N.m_norm, ACT.Tanh).then_inc(s["tanh_taken"], 1)

            def make_numbers():
                N, s = L_numbers, L_s
                for g in range(PERIOD):
                    act.wait_ge(s["x_turned"], g + 1)
                    wait(act, s["projected"], g - 1)
                    a.activation(lifted[:, g % 2, :], ps_turn_L[g % 2], ACT.Copy).then_inc(s["xT_made"], 1)
                    wait(act, s["x_squared"], g - 1)
                    for i in range(UNIT_TILES):
                        t = UNIT_TILES * g + i
                        last = a.activation(lifted_sq[:, g % 2, P * i:P * (i + 1)], x_all[:, t, :], ACT.Square,
                                            accum_out=N.sq[:, t:t + 1])
                    last.then_inc(s["x_squared"], 1)
                act.wait_ge(s["sq_clamped"], 1)
                estimate_root(N, s, "sq_rooted", 0, 2 * N.n)
                take_log(N, s, "log_asked", "log_taken", 0)
                take_tanh(N, s, 0)
                act.wait_ge(s["h_clamped"], 1)
                estimate_root(N, s, "h_rooted", 1, N.n)
                take_log(N, s, "h_log_asked", "h_log_taken", 0)
                act.wait_ge(s["scale_made"], 1)

            def bias_rows(w):
                wait(act, L_exact_made, w - 1)
                for i in range(UNIT_TILES):
                    t = UNIT_TILES * w + i
                    last = a.activation(side[:, t % TILES, :], b_embed[:, :], ACT.Copy,
                                        scale=L_numbers.c_b[:, t:t + 1])
                last.then_inc(bias_rows_made, 1)

            def high_L(w):
                if KINDS[w] != "M":
                    act.wait_ge(L_exact_made, w + 1)
                    a.activation(L_high[:, L_slots(w), :], L_tiles(w), ACT.Copy).then_inc(L_high_made, 1)

            def lift_block(b, j):
                act.wait_ge(half_multiplied, HALVES * PERIOD * (b + 1))
                wait(act, block_projected, b)
                a.activation(lifted[:, 0, :], acc[j], ACT.Copy)
                a.activation(lifted_sq[:, 0, :], acc[j], ACT.Square).then_inc(block_copied, 1)

            def front(f):
                s = pair_s

                def load_x():
                    if isinstance(f, int) and f == 0:
                        act.wait_ge(L_exact_made, PERIOD)
                    else:
                        act.wait_ge(s["res_made"], f)
                    act.dma_start(x_rows[:, :, :].rearrange("p (j t) f -> p j t f", j=2), x_pair[f])\
                        .then_inc(s["x_landed"], DMA)

                def lift_x(j):
                    act.wait_ge(s["x_turned"], 2 * f + j + 1)
                    wait(act, s["projected"], 2 * f + j)
                    a.activation(lifted[:, 1, :], ps_turn, ACT.Copy)
                    a.activation(lifted_sq[:, 1, :], ps_turn, ACT.Square).then_inc(s["xT_made"], 1)

                def copy_products():
                    act.wait_ge(s["projected"], 2 * f + 2)
                    wait(act, s["res_made"], f)
                    a.activation(side[:, :, :].rearrange("p t f -> p (t f)"),
                                 psum[:, 4:6, :].rearrange("p j c -> p (j c)"), ACT.Copy)\
                        .then_inc(s["products_copied"], 1)

                return hooks_of(FRONT_ACT, (
                    ("load_x", load_x), ("copy_0", lambda: lift_x(0)), ("copy_1", lambda: lift_x(1)),
                    ("copy_products", copy_products), ("even", lambda: lift_block(2 * f, 0))))

            def back(f):
                s, N = pair_s, pair_numbers
                n = TILES

                def v_rooted():
                    act.wait_ge(s["v_clamped"], f + 1)
                    estimate_root(N, s, "v_rooted", PAIR_ROOTS * f, n)

                def v_tanh():
                    act.wait_ge(s["v_normed"], f + 1)
                    a.activation(N.th, N.norm[:, 0:n], ACT.Tanh).then_inc(s["v_tanh"], 1)

                def square_y():
                    act.wait_ge(s["y_made"], f + 1)
                    for t in range(n):
                        wait(act, s["squared"], n * f + max(t - 1, 0))
                        a.activation(spare[:, t % 2, :], y_rows[:, t, :], ACT.Square,
                                     accum_out=N.sq[:, n + t:n + t + 1]).then_inc(s["squared"], 1)

                def rooted():
                    act.wait_ge(s["sq_clamped"], f + 1)
                    estimate_root(N, s, "sq_rooted", PAIR_ROOTS * f + 1, 2 * n)

                def scale_bias():
                    act.wait_ge(s["coefs_made"], f + 1)
                    for t in range(n):
                        last = a.activation(side[:, t, :], b_layer[:, :], ACT.Copy, scale=N.c_b[:, t:t + 1])
                    last.then_inc(s["bias_scaled"], 1)

                def var_rooted():
                    act.wait_ge(s["var_clamped"], f + 1)
                    estimate_root(N, s, "var_rooted", PAIR_ROOTS * f + 2, n)

                def store():
                    act.wait_ge(s["shift_made"], f + 1)
                    for t in range(n):
                        last = a.activation(y_rows[:, t, :], y_rows[:, t, :], ACT.Identity, bias=N.tmp[:, t:t + 1],
                                            scale=N.rsq[:, t:t + 1])
                    last.then_inc(s["out_made"], 1)
                    act.wait_ge(s["out_made"], f + 1)
                    act.dma_start(out_pair[f], y_rows[:, :, :].rearrange("p (j t) f -> p j t f", j=2))\
                        .then_inc(s["stored"], DMA)

                return hooks_of(BACK_ACT, (
                    ("odd", lambda: lift_block(2 * f + 1, 1)), ("v_rooted", v_rooted), ("v_tanh", v_tanh),
                    ("square_y", square_y), ("rooted", rooted),
                    ("log", lambda: take_log(N, s, "log_asked", "log_taken", f)),
                    ("tanh", lambda: take_tanh(N, s, f)), ("scale_bias", scale_bias), ("var_rooted", var_rooted),
                    ("store", store)))

            act.dma_start(w_embed[:, 0:D], embed).then_inc(consts_in, DMA)
            act.dma_start(b_embed[:, :], embed_bias.rearrange("(a n) -> a n", a=1).to_broadcast([P, D]))\
                .then_inc(consts_in, DMA)
            act.dma_start(b_layer[:, :], layer_bias.rearrange("(a n) -> a n", a=1).to_broadcast([P, D]))\
                .then_inc(consts_in, DMA)
            act.dma_start(w_x[:, :], layer[0:P, :]).then_inc(consts_in, DMA)
            act.dma_start(w_v[:, :], layer[P:2 * P, :]).then_inc(consts_in, DMA)
            make_numbers()
            bias_rows(0)
            bias_rows(1)
            high_L(0)
            L_hooks = []
            for w in range(PERIOD):
                if w + 2 < PERIOD:
                    L_hooks.append((w, lambda w=w: bias_rows(w + 2)))
                if w + 1 < PERIOD:
                    L_hooks.append((w, lambda w=w: high_L(w + 1)))
            schedule(nc.scalar, blocks, front, back, L_hooks)
            act.wait_ge(pair_s["stored"], DMA * PAIRS)

        @block.gpsimd
        def _(pool):
            g = nc.gpsimd
            g.memset(ident[:, :], 0.0).then_inc(ident_zero, 1)
            pool.wait_ge(ident_zero, 1)
            g.affine_select(out=ident[:, :], in_=ident[:, :], compare_op=ALU.not_equal, fill=1.0, base=0,
                            pattern=[[-1, P]], channel_multiplier=1).then_inc(consts_set, 1)

            def low_L(w):
                if KINDS[w] != "M":
                    pool.wait_ge(L_high_made, ORDER[w] + 1)
                    g.tensor_tensor(L_low[:, L_slots(w), :], L_tiles(w), L_high[:, L_slots(w), :].bitcast(F32),
                                    ALU.subtract).then_inc(L_low_made, 1)

            def blocks(m, hooks):
                for j in range(2):
                    b = 2 * m + j
                    for w in range(PERIOD):
                        if KINDS[w] == "S":
                            slot = place(j, w)[0]
                            for _, n, cols, high in halves_of(w):
                                pool.wait_ge(high_made, HALVES * len(SPLIT) * b + n + 1)
                                g.tensor_tensor(a_low[slot][:, :, cols], a_in[slot][:, :, cols],
                                                a_high[:, high].bitcast(F32), ALU.subtract)\
                                    .then_inc(low_made["S"], 1)
                        run(hooks, PERIOD * j + w)

            low_L(0)
            schedule(nc.gpsimd, blocks, nothing, nothing,
                     [(w - 1, lambda w=w: low_L(w)) for w in range(1, PERIOD)])

        @block.tensor
        def _(pe):
            t_e = nc.tensor

            def blocks(m, hooks):
                for j in range(2):
                    b = 2 * m + j
                    bank = acc[j].rearrange("p (g r) -> p g r", r=R)
                    for w in range(PERIOD):
                        if w == 0:
                            wait(pe, block_copied, b - 1)
                        at_start = isinstance(b, int) and b == 0
                        slot, at = place(j, w)
                        if KINDS[w] == "M":
                            if at_start:
                                pe.wait_ge(L_exact_made, w + 1)
                            pe.wait_ge(unit_turned, PERIOD * b + w + 1)
                            for i in range(UNIT_TILES):
                                last = t_e.matmul(bank, L_whole[:, UNIT_TILES * OF_KIND[w] + i, :],
                                                  a_in[slot][:, :, at + R * i:at + R * (i + 1)],
                                                  start=False, stop=w == PERIOD - 1 and i == UNIT_TILES - 1)
                            last.then_inc(half_multiplied, HALVES)
                        else:
                            if at_start:
                                pe.wait_ge(L_low_made, ORDER[w] + 1)
                            of_kind = HALVES * (KINDS.count(KINDS[w]) * b + OF_KIND[w])
                            for e, _, cols, high_slot in halves_of(w):
                                pe.wait_ge(low_made[KINDS[w]], of_kind + e + 1)
                                for i in range(HALF):
                                    tile = UNIT_TILES * ORDER[w] + HALF * e + i
                                    low = a_low[slot][:, :, cols.start + R * i:cols.start + R * (i + 1)]
                                    high = a_high[:, high_slot, :, R * i:R * (i + 1)]
                                    first = w == 0 and e == 0 and i == 0
                                    end = w == PERIOD - 1 and e == HALVES - 1 and i == HALF - 1
                                    t_e.matmul(bank, L_high[:, tile, :], high, start=first, stop=False)
                                    t_e.matmul(bank, L_high[:, tile, :], low, start=False, stop=False)
                                    last = t_e.matmul(bank, L_low[:, tile, :], high, start=False, stop=end)
                                last.then_inc(half_multiplied, 1)
                        run(hooks, PERIOD * j + w)

            def make_numbers():
                s = L_s
                for g in range(PERIOD + 1):
                    if g < PERIOD:
                        if g % (PERIOD // X_PARTS) == 0:
                            pe.wait_ge(x_in[g // (PERIOD // X_PARTS)], QUADS * DMA)
                        wait(pe, s["xT_made"], g - 1)
                        for i in range(UNIT_TILES):
                            last = t_e.transpose(ps_turn_L[g % 2][:, P * i:P * (i + 1)],
                                                 x_all[:, UNIT_TILES * g + i, :], ident[:, :])
                        last.then_inc(s["x_turned"], 1)
                    if g > 0:
                        k = g - 1
                        pe.wait_ge(s["xT_made"], k + 1)
                        wait(pe, s["u_taken"], k - 1)
                        for i in range(UNIT_TILES):
                            last = t_e.matmul(ps_u[k % 2][:, i // 2, i % 2, :], lifted[:, k % 2, P * i:P * (i + 1)],
                                              w_embed[:, :], start=True, stop=True)
                        last.then_inc(s["projected"], 1)

            def turn_x(f, j):
                pe.wait_ge(pair_s["x_landed"], DMA * (f + 1))
                wait(pe, pair_s["xT_made"], 2 * f + j)
                for t in range(4):
                    last = t_e.transpose(ps_turn[:, P * t:P * (t + 1)], x_rows[:, 4 * j + t, :], ident[:, :])
                last.then_inc(pair_s["x_turned"], 1)

            def project_x(f, j):
                pe.wait_ge(pair_s["xT_made"], 2 * f + j + 1)
                wait(pe, pair_s["products_copied"], f)
                wait(pe, pair_s["sums_taken"], f)
                for t in range(4):
                    xT, at = lifted[:, 1, P * t:P * (t + 1)], 2 * TILES + 4 * j + t
                    t_e.matmul(ps_x[4 * j + t], xT, w_x[:, :], start=True, stop=True)
                    t_e.matmul(ps_sum[:, at:at + 1], lifted_sq[:, 1, P * t:P * (t + 1)], ones[:, :],
                               start=True, stop=True)
                    last = t_e.matmul(ps_sum[:, at + TILES:at + TILES + 1], xT, layer_b[:, 0:1],
                                      start=True, stop=True)
                last.then_inc(pair_s["projected"], 1)

            def project_block(f, j):
                pe.wait_ge(block_copied, 2 * f + j + 1)
                wait(pe, pair_s["y_made"], f)
                wait(pe, pair_s["sums_taken"], f)
                vT = lifted[:, 0, :].rearrange("f (p t) -> f t p", t=4)
                v_sqT = lifted_sq[:, 0, :].rearrange("f (p t) -> f t p", t=4)
                for t in range(4):
                    at = 4 * j + t
                    t_e.matmul(ps_v[at], vT[:, t, :], w_v[:, :], start=True, stop=True)
                    t_e.matmul(ps_sum[:, at:at + 1], v_sqT[:, t, :], ones[:, :], start=True, stop=True)
                    last = t_e.matmul(ps_sum[:, TILES + at:TILES + at + 1], vT[:, t, :], layer_b[:, 1:2],
                                      start=True, stop=True)
                last.then_inc(block_projected, 1)

            def front(f):
                return hooks_of(FRONT_PE, (
                    ("turn_0", lambda: turn_x(f, 0)), ("project_0", lambda: project_x(f, 0)),
                    ("turn_1", lambda: turn_x(f, 1)), ("project_1", lambda: project_x(f, 1)),
                    ("even", lambda: project_block(f, 0))))

            def back(f):
                return hooks_of(BACK_PE, (("odd", lambda: project_block(f, 1)),))

            pe.wait_ge(consts_in, 5 * DMA)
            pe.wait_ge(consts_set, 2)
            pe.wait_ge(bias_done, 5)
            make_numbers()
            schedule(nc.tensor, blocks, front, back)


def kernel(x, adj, L0_gnn_embed, L0_gnn_layer, L0_gnn_embed_bias, L0_gnn_layer_bias):
    import numpy as np
    import concourse.bacc as bacc
    from concourse.bass_utils import run_bass_kernel_spmd

    nc = bacc.Bacc("TRN2", target_bir_lowering=False, num_devices=1)
    given = {"x": x, "adj": adj, "embed": L0_gnn_embed, "layer": L0_gnn_layer, "embed_bias": L0_gnn_embed_bias,
             "layer_bias": L0_gnn_layer_bias}
    arrays = {name: np.ascontiguousarray(a) for name, a in given.items()}
    drams = {name: nc.dram_tensor(name, a.shape, mybir.dt.from_np(a.dtype), kind="ExternalInput").ap()
             for name, a in arrays.items()}
    out = nc.dram_tensor("out", arrays["x"].shape, F32, kind="ExternalOutput").ap()
    graph_layer(nc, out=out, **drams)
    result = run_bass_kernel_spmd(nc, [arrays], core_ids=[0])
    return result.results[0]["out"]
```

```python
from contextlib import ExitStack

import concourse.bass as bass
from concourse import mybir

F32 = mybir.dt.float32
F32R = mybir.dt.float32r
ACT = mybir.ActivationFunctionType
ALU = mybir.AluOpType

P = 128
QUADS = 4
R = P // QUADS
EPS = 1e-7
MAX_TANH = 1.0 - 1e-6
LN_EPS = 1e-5

ROWS = 512
GROUPS = ROWS // R
STEP_COLS = 256
UNIT_TILES = 4
UNIT_COLS = UNIT_TILES * R
PERIOD = 16
STEPS = PERIOD // 2
KINDS = "SMSSMMSMSSSMSSMS"
SPLIT = [w for w in range(PERIOD) if KINDS[w] != "M"]
ORDER = {w: n for n, w in enumerate(SPLIT)}
LOW_BY_VECTOR = (26,)
LOW_BEHIND = 4
WHOLE = [w for w in range(PERIOD) if KINDS[w] == "M"]
SLOT_OF_STEP = (0, 1, 2, 3, 4, 0, 5, 6, 3, 1, 0, 2, 4, 3, 5, 6)
IN_SLOTS = 7
STEPS_OF_SLOT = [[s for s in range(2 * STEPS) if SLOT_OF_STEP[s] == slot] for slot in range(IN_SLOTS)]
HALVES = 2
HALF = UNIT_TILES // HALVES
HALF_COLS = HALF * R
H_SLOTS = 5
TILES = 8
ALL_TILES = PERIOD * UNIT_TILES
PART = ALL_TILES // 2
X_PARTS = 4
X_SLOTS = (IN_SLOTS - 2, IN_SLOTS)
DMA = 16

FRONT_PE = dict(turn_0=19, project_0=21, turn_1=20, project_1=25, even=27)
FRONT_ACT = dict(load_x=18, square_x=22, copy_0=20, products_0=25, copy_1=26, products_1=28, even=18)
BACK_PE = dict(odd=0)
BACK_ACT = dict(odd=1, v_rooted=4, v_tanh=5, square_y=7, rooted=9, log=13, tanh=13, scale_bias=16, var_rooted=20,
                store=20)
BACK_DVE = dict(take_sums=7, norm_v=9, y_of_v=9, clamp=10, ask_log=15, ask_tanh=15, coefs=18, residual=19,
                variance=19, shift=21)
L_DVE = (9, 11, 13, 14, 15)
L_ACT = (11, 13, 14, 15, 15)
L_DVE_HOOKS = (0, 1, 2, 3, 4, 5)
L_ACT_HOOKS = (0, 1, 2, 3, 4)
TURNED_EARLY = 1

PAIR_LINKS = 43
PAIR_ROOTS = 3


class Numbers:
    DOUBLE = ("sq", "clamped", "rsq", "norm", "tmp")
    SINGLE = ("lg", "zh", "arg", "rec", "alpha", "th", "dot", "c_y", "c_b", "beta", "m_norm")
    KINDS = 2 * len(DOUBLE) + len(SINGLE)

    def __init__(self, tensor, n):
        views = [tensor[:, n * i:n * (i + 2)] for i in range(0, 2 * len(self.DOUBLE), 2)]
        views += [tensor[:, n * i:n * (i + 1)] for i in range(2 * len(self.DOUBLE), self.KINDS)]
        (self.sq, self.clamped, self.rsq, self.norm, self.tmp, self.lg, self.zh, self.arg, self.rec, self.alpha,
         self.th, self.dot, self.c_y, self.c_b, self.beta, self.m_norm) = views
        self.n = n


def graph_layer(nc, x, adj, embed, layer, embed_bias, layer_bias, out):
    N, D = x.shape
    BLOCKS = adj.shape[0] // ROWS
    PAIRS = BLOCKS // 2
    assert D == P and N // QUADS // UNIT_COLS == PERIOD and STEP_COLS == 2 * UNIT_COLS and BLOCKS % 2 == 0
    assert all(at % PERIOD in SPLIT and at + LOW_BEHIND < 2 * PERIOD for at in LOW_BY_VECTOR)
    assert 2 * len(SPLIT) * HALVES % H_SLOTS == 0

    adj_v = adj.rearrange("(k g r) (q j c) -> k j q r g c", g=GROUPS, r=R, q=QUADS, c=STEP_COLS)
    x_part = x.rearrange("(q n t c) f -> n q c t f", q=QUADS, n=X_PARTS, c=R)
    x_pair = x.rearrange("(m j p t) f -> m p j t f", j=2, p=P, t=4)
    out_pair = out.rearrange("(m j p t) f -> m p j t f", j=2, p=P, t=4)

    with ExitStack() as ctx:
        def sb(name, shape, dt=F32):
            return ctx.enter_context(nc.sbuf_tensor(name, shape, dt))

        def sem(name):
            return ctx.enter_context(nc.semaphore(name))

        def over(name, shape, dt, offset):
            return nc.alloc_sbuf_tensor_at(name, shape, dt, offset=offset)

        def next_place():
            return (nc.sbuf_base + 31) // 32 * 32

        a_in, a_low = [], []
        for i in range(IN_SLOTS):
            if i == X_SLOTS[0]:
                x_all = over("x_all", [P, ALL_TILES, D], F32, next_place())
            a_low.append(over(f"a_low_{i}", [P, GROUPS, STEP_COLS], F32R, next_place()))
            a_in.append(sb(f"a_in_{i}", [P, GROUPS, STEP_COLS]))
        a_high = sb("a_high", [P, H_SLOTS, GROUPS, HALF_COLS], F32R)
        L_high = sb("L_high", [P, len(SPLIT) * UNIT_TILES, D], F32R)
        L_at = next_place()
        L_low = sb("L_low", [P, len(SPLIT) * UNIT_TILES, D], F32R)
        L_exact = over("L_exact", [P, len(SPLIT) * UNIT_TILES, D], F32, L_at)
        L_whole = sb("L_whole", [P, (PERIOD - len(SPLIT)) * UNIT_TILES, D])
        rows_at = next_place()
        x_rows = sb("x_rows", [P, TILES, D])
        y_rows = sb("y_rows", [P, TILES, D])
        side = sb("side", [P, TILES, D + 1])
        lifted = sb("lifted", [P, 2, ROWS])
        v_sqT = sb("v_sqT", [P, ROWS])
        embed_at = next_place()
        w_embed = sb("w_embed", [P, D + 1])
        b_embed = sb("b_embed", [P, D])
        w_x = sb("w_x", [P, D + 1])
        w_v = sb("w_v", [P, D + 1])
        b_layer = sb("b_layer", [P, D])
        ident = sb("ident", [P, P])
        ones = sb("ones", [P, 1])
        b_sq = sb("b_sq", [P, 2])
        pair_numbers = Numbers(sb("pair_numbers", [P, Numbers.KINDS * TILES]), TILES)
        L_numbers = [Numbers(over(f"L_numbers_{p}", [P, Numbers.KINDS * PART], F32,
                                  rows_at + 4 * TILES * D * p), PART) for p in range(2)]
        assert Numbers.KINDS * PART <= TILES * D
        spare = sb("spare", [P, TILES, D], mybir.dt.bfloat16)
        bias_at = embed_at + 4 * (D + 1) + 28
        sums = over("sums", [P, 3 * TILES], F32, bias_at)
        stats = over("stats", [P, TILES, 6], F32, bias_at + 4 * 4 * TILES)
        mean_sum = over("mean_sum", [P, TILES], F32, bias_at + 4 * 10 * TILES)

        psum = ctx.enter_context(nc.psum_tensor("psum", [P, 8, ROWS], F32))
        acc = [psum[:, j, :] for j in range(2)]
        ps_v = [psum[:, 2 + t // 3, (D + 1) * (t % 3):(D + 1) * (t % 3 + 1)] for t in range(TILES)]
        ps_v_sq = psum[:, 2 + TILES // 3, (D + 1) * (TILES % 3):(D + 1) * (TILES % 3) + TILES]
        ps_x = psum[:, 5:7, 0:2 * (D + 1)].rearrange("p k (t c) -> p k t c", t=2)
        ps_turn = psum[:, 7, :]
        ps_turn_L = [psum[:, j, :] for j in range(2)]
        ps_u = [psum[:, 2 + 2 * j:4 + 2 * j, 0:2 * (D + 1)].rearrange("p k (t c) -> p k t c", t=2) for j in range(2)]

        consts_in, ident_zero, consts_set, bias_done = (
            sem(n) for n in ("consts_in", "ident_zero", "consts_set", "bias_done"))
        x_in = [sem(f"x_in_{n}") for n in range(X_PARTS)]
        step_landed = [sem(f"step_landed_{i}") for i in range(IN_SLOTS)]
        unit_turned, high_made, half_multiplied = sem("unit_turned"), sem("high_made"), sem("half_multiplied")
        low_by_pool, low_by_vector = sem("low_by_pool"), sem("low_by_vector")
        block_copied, block_projected = sem("block_copied"), sem("block_projected")
        bias_rows_made, L_exact_made, L_high_made, L_low_made = (
            sem(n) for n in ("bias_rows_made", "L_exact_made", "L_high_made", "L_low_made"))
        COMMON = ("x_turned", "xT_made", "projected", "sq_clamped", "sq_rooted", "log_asked", "log_taken",
                  "tanh_asked", "tanh_taken", "coefs_made", "dve_step", "act_step")
        L_s = {n: sem(f"L_{n}") for n in COMMON + (
            "x_squared", "u_taken", "u_squared", "h_clamped", "h_rooted", "h_log_asked", "h_log_taken", "scale_made")}
        pair_s = {n: sem(f"pair_{n}") for n in COMMON + (
            "x_landed", "products_copied", "sums_taken", "v_clamped", "v_rooted", "v_normed", "v_tanh", "y_made",
            "squared", "bias_scaled", "res_made", "var_clamped", "var_rooted", "shift_made", "out_made", "stored")}

        block = ctx.enter_context(nc.Block())

        def wait(eng, s, value):
            if not isinstance(value, int) or value > 0:
                eng.wait_ge(s, value)

        def high_free(m, n):
            pairs_back = 1 if n < H_SLOTS else 0
            j, last = divmod(n - H_SLOTS + pairs_back * 2 * HALVES * len(SPLIT), HALVES * len(SPLIT))
            unit = PERIOD * j + SPLIT[last // HALVES]
            return HALVES * (2 * PERIOD * (m - pairs_back) + unit) + last % HALVES + 1

        def place(j, w):
            return SLOT_OF_STEP[STEPS * j + w // 2], UNIT_COLS * (w % 2)

        def halves_of(j, w):
            at = UNIT_COLS * (w % 2)
            for e in range(HALVES):
                n = HALVES * (len(SPLIT) * j + ORDER[w]) + e
                yield e, n, slice(at + HALF_COLS * e, at + HALF_COLS * (e + 1)), n % H_SLOTS

        def low_made(m, j, w, e):
            at = PERIOD * j + w
            by_vector = at in LOW_BY_VECTOR
            units = [PERIOD * i + k for i in range(2) for k in SPLIT if (PERIOD * i + k in LOW_BY_VECTOR) == by_vector]
            return low_by_vector if by_vector else low_by_pool, HALVES * (len(units) * m + units.index(at)) + e + 1

        def L_tiles(w):
            if KINDS[w] == "M":
                return L_whole[:, UNIT_TILES * WHOLE.index(w):UNIT_TILES * (WHOLE.index(w) + 1), :]
            return L_exact[:, UNIT_TILES * ORDER[w]:UNIT_TILES * (ORDER[w] + 1), :]

        def L_slots(w):
            return slice(UNIT_TILES * ORDER[w], UNIT_TILES * (ORDER[w] + 1))

        def steps_of(eng, s, base):
            done = [0]

            def step(ins):
                ins.then_inc(s, 1)
                done[0] += 1
                eng.wait_ge(s, base + done[0])
            step.done = done
            return step

        def run(hooks, w):
            for at, action in hooks:
                if at == w:
                    action()

        def hooks_of(slots, actions):
            return [(slots[name], action) for name, action in actions]

        def schedule(engine, blocks, front, back, L_hooks=()):
            blocks(0, list(L_hooks) + front(0))
            blocks(1, back(0) + front(1))
            with engine.Fori(2, PAIRS) as m:
                blocks(m, back(m - 1) + front(m))
            for _, action in back(PAIRS - 1):
                action()

        def nothing(f):
            return []

        @block.sync
        def _(sp):
            for n in range(X_PARTS):
                tiles = slice(ALL_TILES // X_PARTS * n, ALL_TILES // X_PARTS * (n + 1))
                for q in range(QUADS):
                    sp.dma_start(x_all[R * q:R * (q + 1), tiles, :], x_part[n, q]).then_inc(x_in[n], DMA)
            sp.wait_ge(x_in[X_PARTS - 2], QUADS * DMA)

            def blocks(m, hooks):
                for s in range(2 * STEPS):
                    slot = SLOT_OF_STEP[s]
                    n = STEPS_OF_SLOT[slot].index(s)
                    last = STEPS_OF_SLOT[slot][n - 1] - (2 * STEPS if n == 0 else 0)
                    wait(sp, half_multiplied, HALVES * (2 * PERIOD * m + 2 * last + 2))
                    if isinstance(m, int) and m == 0 and n == 0 and slot in range(*X_SLOTS):
                        sp.wait_ge(L_s["x_turned"], PERIOD)
                        sp.wait_ge(L_s["x_squared"], PERIOD)
                    for q in range(QUADS):
                        sp.dma_start(a_in[slot][R * q:R * (q + 1)], adj_v[2 * m + s // STEPS, s % STEPS, q])\
                            .then_inc(step_landed[slot], DMA)

            schedule(nc.sync, blocks, nothing, nothing)

        @block.vector
        def _(dve):
            v = nc.vector

            def turn(m, j, w):
                slot, at = place(j, w)
                users = STEPS_OF_SLOT[slot]
                uses = len(users) * m + users.index(STEPS * j + w // 2) + 1
                dve.wait_ge(step_landed[slot], QUADS * DMA * uses)
                unit = a_in[slot][:, :, at:at + UNIT_COLS]
                v.transpose(unit, unit).then_inc(unit_turned, 1)

            def low(m, at):
                j, w = divmod(at, PERIOD)
                slot = place(j, w)[0]
                for _, n, cols, high in halves_of(j, w):
                    dve.wait_ge(high_made, HALVES * 2 * len(SPLIT) * m + n + 1)
                    v.tensor_tensor(a_low[slot][:, :, cols], a_in[slot][:, :, cols], a_high[:, high].bitcast(F32),
                                    ALU.subtract).then_inc(low_by_vector, 1)

            def blocks(m, hooks):
                for j in range(2):
                    for w in range(PERIOD):
                        at_start = isinstance(m, int) and m == 0 and j == 0
                        if not (at_start and w < TURNED_EARLY):
                            turn(m, j, w)
                        if PERIOD * j + w - LOW_BEHIND in LOW_BY_VECTOR:
                            low(m, PERIOD * j + w - LOW_BEHIND)
                        run(hooks, PERIOD * j + w)

            def root(N, step, n):
                tmp, rsq, clamped = N.tmp[:, 0:n], N.rsq[:, 0:n], N.clamped[:, 0:n]
                step(v.tensor_tensor(tmp, rsq, rsq, ALU.mult))
                step(v.tensor_tensor(tmp, tmp, clamped, ALU.mult))
                step(v.tensor_scalar(tmp, tmp, -0.5, 1.5, ALU.mult, ALU.add))
                step(v.tensor_tensor(rsq, rsq, tmp, ALU.mult))
                return v.tensor_tensor(N.norm[:, 0:n], clamped, rsq, ALU.mult)

            def log_argument(N, step):
                step(v.tensor_scalar(N.zh, N.norm[:, 0:N.n], MAX_TANH, None, ALU.min))
                step(v.tensor_scalar(N.arg, N.zh, -1.0, 1.0, ALU.mult, ALU.add))
                step(v.reciprocal(N.rec, N.arg))
                step(v.tensor_tensor(N.zh, N.zh, N.rec, ALU.mult))
                return v.tensor_scalar(N.arg, N.zh, 2.0, 1.0, ALU.mult, ALU.add)

            def artanh_over_norm(N, step):
                step(v.tensor_scalar(N.arg, N.arg, 1.0, None, ALU.subtract))
                step(v.reciprocal(N.rec, N.arg))
                step(v.tensor_tensor(N.zh, N.zh, N.lg, ALU.mult))
                step(v.tensor_tensor(N.zh, N.zh, N.rec, ALU.mult))
                return v.tensor_tensor(N.alpha, N.zh, N.rsq[:, 0:N.n], ALU.mult)

            def ask_log(N, step, s, count):
                dve.wait_ge(s["sq_rooted"], count + 1)
                step(root(N, step, 2 * N.n))
                log_argument(N, step).then_inc(s["log_asked"], 1)
                dve.wait_ge(s["log_asked"], count + 1)

            def ask_tanh(N, step, s, count):
                dve.wait_ge(s["log_taken"], count + 1)
                step(artanh_over_norm(N, step))
                step(v.tensor_tensor(N.m_norm, N.alpha, N.norm[:, N.n:2 * N.n], ALU.mult))
                v.tensor_scalar(N.m_norm, N.m_norm, EPS, None, ALU.max).then_inc(s["tanh_asked"], 1)
                dve.wait_ge(s["tanh_asked"], count + 1)

            def coefs(N, step, s, count, bb):
                x2, y_sq = N.tmp[:, 0:N.n], N.sq[:, N.n:2 * N.n]
                double = N.tmp[:, N.n:2 * N.n]
                dve.wait_ge(s["tanh_taken"], count + 1)
                step(v.reciprocal(N.rec, N.m_norm))
                step(v.tensor_tensor(N.beta, N.th, N.rec, ALU.mult))
                step(v.tensor_tensor(N.beta, N.beta, N.alpha, ALU.mult))
                v.tensor_tensor(double, N.dot, N.beta, ALU.mult)
                step(v.tensor_tensor(x2, N.beta, N.beta, ALU.mult))
                v.tensor_scalar(double, double, 2.0, 1.0, ALU.mult, ALU.add)
                step(v.tensor_tensor(x2, x2, y_sq, ALU.mult))
                step(v.scalar_tensor_tensor(out=N.c_b, in0=x2, scalar=bb, in1=double, op0=ALU.mult, op1=ALU.add))
                step(v.tensor_scalar(N.c_b, N.c_b, EPS, None, ALU.max))
                step(v.reciprocal(N.rec, N.c_b))
                v.scalar_tensor_tensor(out=N.c_y, in0=double, scalar=bb, in1=N.beta, op0=ALU.add, op1=ALU.mult)
                step(v.tensor_scalar(x2, x2, -1.0, 1.0, ALU.mult, ALU.add))
                v.tensor_tensor(N.c_y, N.c_y, N.rec, ALU.mult)
                v.tensor_tensor(N.c_b, x2, N.rec, ALU.mult).then_inc(s["coefs_made"], 1)
                dve.wait_ge(s["coefs_made"], count + 1)

            def take_u(g):
                N, s = L_numbers[g // (PERIOD // 2)], L_s
                first = UNIT_TILES * (g % (PERIOD // 2))
                dve.wait_ge(s["projected"], g + 1)
                u_rows = L_tiles(g).rearrange("p (k t) f -> p k t f", k=2)
                dots = N.dot[:, first:first + UNIT_TILES].rearrange("p (k t) -> p k t", k=2)
                v.tensor_copy(dots, ps_u[g % 2][:, :, :, D])
                v.tensor_copy(u_rows, ps_u[g % 2][:, :, :, 0:D]).then_inc(s["u_taken"], 1)
                dve.wait_ge(s["u_taken"], g + 1)
                for i in range(UNIT_TILES):
                    u, total = L_tiles(g)[:, i, :], N.n + first + i
                    last = v.tensor_tensor_reduce(out=side[:, (first + i) % TILES, 0:D], in0=u, in1=u, scale=1.0,
                                                  scalar=0.0, op0=ALU.mult, op1=ALU.add,
                                                  accum_out=N.sq[:, total:total + 1])
                last.then_inc(s["u_squared"], 1)

            L_step = steps_of(dve, L_s["dve_step"], 0)

            def number_stages(p):
                N, s, step, n = L_numbers[p], L_s, L_step, PART

                def clamp():
                    dve.wait_ge(s["u_squared"], PERIOD // 2 * (p + 1))
                    dve.wait_ge(s["x_squared"], PERIOD // 2 * (p + 1))
                    v.tensor_scalar(N.clamped, N.sq, EPS * EPS, None, ALU.max).then_inc(s["sq_clamped"], 1)

                def coefs_and_h():
                    coefs(N, step, s, p, b_sq[:, 0:1])
                    h_sq, rest = N.clamped[:, 0:n], N.clamped[:, n:2 * n]
                    v.tensor_tensor(h_sq, N.c_y, N.sq[:, n:2 * n], ALU.mult)
                    step(v.tensor_tensor(rest, N.c_b, N.dot, ALU.mult))
                    step(v.scalar_tensor_tensor(out=h_sq, in0=rest, scalar=2.0, in1=h_sq, op0=ALU.mult, op1=ALU.add))
                    v.tensor_tensor(h_sq, h_sq, N.c_y, ALU.mult)
                    step(v.tensor_tensor(rest, N.c_b, N.c_b, ALU.mult))
                    step(v.scalar_tensor_tensor(out=h_sq, in0=rest, scalar=b_sq[:, 0:1], in1=h_sq,
                                                op0=ALU.mult, op1=ALU.add))
                    v.tensor_scalar(h_sq, h_sq, EPS * EPS, None, ALU.max).then_inc(s["h_clamped"], 1)

                def ask_h_log():
                    dve.wait_ge(s["h_rooted"], p + 1)
                    step(root(N, step, n))
                    log_argument(N, step).then_inc(s["h_log_asked"], 1)
                    dve.wait_ge(s["h_log_asked"], p + 1)

                def scale():
                    dve.wait_ge(s["h_log_taken"], p + 1)
                    step(artanh_over_norm(N, step))
                    v.tensor_tensor(N.c_b, N.c_b, N.alpha, ALU.mult)
                    v.tensor_tensor(N.c_y, N.c_y, N.alpha, ALU.mult).then_inc(s["scale_made"], 1)
                    dve.wait_ge(s["scale_made"], p + 1)

                return (clamp, lambda: ask_log(N, step, s, p), lambda: ask_tanh(N, step, s, p), coefs_and_h,
                        ask_h_log, scale)

            def L_rows(w):
                c_y = L_numbers[UNIT_TILES * w // PART].c_y
                dve.wait_ge(bias_rows_made, w + 1)
                for i in range(UNIT_TILES):
                    t, row = (UNIT_TILES * w + i) % PART, L_tiles(w)[:, i, :]
                    last = v.scalar_tensor_tensor(out=row, in0=row, scalar=c_y[:, t:t + 1],
                                                  in1=side[:, t % TILES, 0:D], op0=ALU.mult, op1=ALU.add)
                last.then_inc(L_exact_made, 1)

            def low_L(w):
                if KINDS[w] != "M":
                    dve.wait_ge(L_high_made, ORDER[w] + 1)
                    v.tensor_tensor(L_low[:, L_slots(w), :], L_tiles(w), L_high[:, L_slots(w), :].bitcast(F32),
                                    ALU.subtract).then_inc(L_low_made, 1)

            def back(f):
                s, N, step = pair_s, pair_numbers, steps_of(dve, pair_s["dve_step"], f * PAIR_LINKS)
                n = TILES
                v_sq, v_dot, x_sq = (sums[:, n * i:n * (i + 1)] for i in range(3))

                def take_sums():
                    dve.wait_ge(block_projected, 2 * f + 2)
                    v.tensor_copy(v_sq, ps_v_sq)
                    for k in range(3):
                        dots = slice(3 * k, min(3 * (k + 1), n))
                        last = v.tensor_copy(v_dot[:, dots], psum[:, 2 + k, 0:3 * (D + 1)].rearrange(
                            "p (t c) -> p t c", t=3)[:, 0:dots.stop - dots.start, D])
                    last.then_inc(s["sums_taken"], 1)
                    dve.wait_ge(s["sums_taken"], f + 1)
                    v.tensor_scalar(N.clamped[:, 0:n], v_sq, EPS * EPS, None, ALU.max).then_inc(s["v_clamped"], 1)

                def norm_v():
                    dve.wait_ge(s["v_rooted"], f + 1)
                    root(N, step, n).then_inc(s["v_normed"], 1)
                    dve.wait_ge(s["v_normed"], f + 1)

                def y_of_v():
                    x2, rest = N.tmp[:, 0:n], N.tmp[:, n:2 * n]
                    dve.wait_ge(s["v_tanh"], f + 1)
                    step(v.tensor_tensor(N.th, N.th, N.rsq[:, 0:n], ALU.mult))
                    dve.wait_ge(s["products_copied"], 2 * (f + 1))
                    wait(dve, s["stored"], DMA * f)
                    for t in range(n):
                        last = v.scalar_tensor_tensor(out=y_rows[:, t, :], in0=ps_v[t][:, 0:D],
                                                      scalar=N.th[:, t:t + 1], in1=side[:, t, 0:D],
                                                      op0=ALU.mult, op1=ALU.add)
                        if t % 4 == 3:
                            last.then_inc(s["y_made"], 1)
                    v.tensor_tensor(rest, N.th, v_dot, ALU.mult)
                    dve.wait_ge(s["squared"], 2 * f + 1)
                    step(v.tensor_tensor(x2, N.th, N.th, ALU.mult))
                    v.tensor_tensor(N.dot, side[:, :, D], rest, ALU.add)
                    step(v.tensor_tensor(x2, x2, v_sq, ALU.mult))
                    step(v.tensor_tensor(N.sq[:, 0:n], x_sq, x2, ALU.add))

                def clamp():
                    dve.wait_ge(s["squared"], 2 * (f + 1))
                    v.tensor_scalar(N.clamped, N.sq, EPS * EPS, None, ALU.max).then_inc(s["sq_clamped"], 1)

                def residual():
                    for j in range(2):
                        half = slice(4 * j, 4 * j + 4)
                        dve.wait_ge(s["bias_scaled"], 2 * f + j + 1)
                        step(v.tensor_tensor(side[:, half, 0:D], side[:, half, 0:D], x_rows[:, half, :], ALU.add))
                        for t in range(4 * j, 4 * j + 4):
                            last = v.scalar_tensor_tensor(out=y_rows[:, t, :], in0=y_rows[:, t, :],
                                                          scalar=N.c_y[:, t:t + 1], in1=side[:, t, 0:D],
                                                          op0=ALU.mult, op1=ALU.add)
                    last.then_inc(s["res_made"], 1)

                def variance():
                    dve.wait_ge(s["res_made"], f + 1)
                    for t in range(n):
                        last = v.bn_stats(stats[:, t, :], y_rows[:, t, :])
                    step(last)
                    mean_0, mean_1, cv_0, cv_1 = (stats[:, :, i] for i in (1, 4, 2, 5))
                    v.tensor_tensor(mean_sum[:, :], mean_0, mean_1, ALU.add)
                    v.tensor_tensor(N.zh, cv_0, cv_1, ALU.add)
                    step(v.tensor_tensor(N.arg, mean_0, mean_1, ALU.subtract))
                    step(v.tensor_tensor(N.arg, N.arg, N.arg, ALU.mult))
                    step(v.scalar_tensor_tensor(out=N.zh, in0=N.arg, scalar=D / 4.0, in1=N.zh,
                                                op0=ALU.mult, op1=ALU.add))
                    v.tensor_scalar(N.clamped[:, 0:n], N.zh, 1.0 / D, LN_EPS, ALU.mult, ALU.add)\
                        .then_inc(s["var_clamped"], 1)

                def shift():
                    dve.wait_ge(s["var_rooted"], f + 1)
                    step(root(N, step, n))
                    v.scalar_tensor_tensor(out=N.tmp[:, 0:n], in0=mean_sum[:, :], scalar=-0.5,
                                           in1=N.rsq[:, 0:n], op0=ALU.mult, op1=ALU.mult)\
                        .then_inc(s["shift_made"], 1)
                    assert step.done[0] == PAIR_LINKS, step.done

                return hooks_of(BACK_DVE, (
                    ("take_sums", take_sums), ("norm_v", norm_v), ("y_of_v", y_of_v), ("clamp", clamp),
                    ("ask_log", lambda: ask_log(N, step, s, f)), ("ask_tanh", lambda: ask_tanh(N, step, s, f)),
                    ("coefs", lambda: coefs(N, step, s, f, b_sq[:, 1:2])), ("residual", residual),
                    ("variance", variance), ("shift", shift)))

            v.memset(ones[:, :], 1.0).then_inc(consts_set, 1)
            dve.wait_ge(consts_in, 5 * DMA)
            for i, (a, b, total) in enumerate(((b_embed, b_embed, b_sq[:, 0:1]), (b_layer, b_layer, b_sq[:, 1:2]),
                                               (w_embed, b_embed, w_embed[:, D:D + 1]),
                                               (w_x, b_layer, w_x[:, D:D + 1]),
                                               (w_v, b_layer, w_v[:, D:D + 1]))):
                v.tensor_tensor_reduce(out=side[:, i, 0:D], in0=a[:, 0:D], in1=b[:, :], scale=1.0, scalar=0.0,
                                       op0=ALU.mult, op1=ALU.add, accum_out=total).then_inc(bias_done, 1)
            dve.wait_ge(bias_done, 5)
            first, second = number_stages(0), number_stages(1)
            for g in range(PERIOD):
                take_u(g)
                run(zip(L_DVE, first), g)
            for w in range(TURNED_EARLY):
                turn(0, 0, w)
            first[-1]()
            L_rows(0)
            L_hooks = list(zip(L_DVE_HOOKS, second))
            for w in range(PERIOD):
                if w + 1 < PERIOD:
                    L_hooks.append((w, lambda w=w: L_rows(w + 1)))
                L_hooks.append((w, lambda w=w: low_L(w)))
            schedule(nc.vector, blocks, nothing, back, L_hooks)

        @block.scalar
        def _(act):
            a = nc.scalar

            def blocks(m, hooks):
                for j in range(2):
                    b = 2 * m + j
                    for w in range(PERIOD):
                        if KINDS[w] != "M":
                            act.wait_ge(unit_turned, PERIOD * b + w + 1)
                            for _, n, cols, high in halves_of(j, w):
                                wait(act, half_multiplied, high_free(m, n))
                                a.activation(a_high[:, high], a_in[place(j, w)[0]][:, :, cols], ACT.Copy)\
                                    .then_inc(high_made, 1)
                        run(hooks, PERIOD * j + w)

            def estimate_root(N, s, name, base, n):
                step = steps_of(act, s["act_step"], base)
                step(a.activation(N.rsq[:, 0:n], N.clamped[:, 0:n], ACT.Ln))
                a.activation(N.rsq[:, 0:n], N.rsq[:, 0:n], ACT.Exp, scale=-0.5).then_inc(s[name], 1)

            def take_log(N, s, asked, taken, count):
                act.wait_ge(s[asked], count + 1)
                a.activation(N.lg, N.arg, ACT.Ln).then_inc(s[taken], 1)

            def take_tanh(N, s, count):
                act.wait_ge(s["tanh_asked"], count + 1)
                a.activation(N.th, N.m_norm, ACT.Tanh).then_inc(s["tanh_taken"], 1)

            def take_x(g):
                N, s = L_numbers[g // (PERIOD // 2)], L_s
                act.wait_ge(s["x_turned"], g + 1)
                wait(act, s["projected"], g - 1)
                a.activation(lifted[:, g % 2, :], ps_turn_L[g % 2], ACT.Copy).then_inc(s["xT_made"], 1)
                wait(act, s["x_squared"], g)
                for i in range(UNIT_TILES):
                    t = UNIT_TILES * g + i
                    last = a.activation(v_sqT[:, P * i:P * (i + 1)], x_all[:, t, :], ACT.Square,
                                        accum_out=N.sq[:, t % PART:t % PART + 1])
                last.then_inc(s["x_squared"], 1)

            def number_stages(p):
                N, s = L_numbers[p], L_s

                def rooted():
                    act.wait_ge(s["sq_clamped"], p + 1)
                    estimate_root(N, s, "sq_rooted", 2 * p, 2 * N.n)

                def h_rooted():
                    act.wait_ge(s["h_clamped"], p + 1)
                    estimate_root(N, s, "h_rooted", 2 * p + 1, N.n)

                return (rooted, lambda: take_log(N, s, "log_asked", "log_taken", p), lambda: take_tanh(N, s, p),
                        h_rooted, lambda: take_log(N, s, "h_log_asked", "h_log_taken", p))

            def bias_rows(w):
                c_b = L_numbers[UNIT_TILES * w // PART].c_b
                act.wait_ge(L_s["scale_made"], UNIT_TILES * w // PART + 1)
                wait(act, L_exact_made, w - 1)
                for i in range(UNIT_TILES):
                    t = UNIT_TILES * w + i
                    last = a.activation(side[:, t % TILES, 0:D], b_embed[:, :], ACT.Copy,
                                        scale=c_b[:, t % PART:t % PART + 1])
                last.then_inc(bias_rows_made, 1)

            def high_L(w):
                if KINDS[w] != "M":
                    act.wait_ge(L_exact_made, w + 1)
                    a.activation(L_high[:, L_slots(w), :], L_tiles(w), ACT.Copy).then_inc(L_high_made, 1)

            def lift_block(b, j):
                act.wait_ge(half_multiplied, HALVES * PERIOD * (b + 1))
                wait(act, block_projected, b)
                a.activation(lifted[:, 0, :], acc[j], ACT.Copy)
                a.activation(v_sqT[:, :], acc[j], ACT.Square).then_inc(block_copied, 1)

            def squares(s, count, rows, totals, tiles):
                wait(act, s["squared"], count)
                for t in tiles:
                    last = a.activation(spare[:, t, :], rows[:, t, :], ACT.Square, accum_out=totals[:, t:t + 1])
                return last

            def front(f):
                s, n = pair_s, TILES

                def load_x():
                    if isinstance(f, int) and f == 0:
                        act.wait_ge(L_exact_made, PERIOD)
                    else:
                        act.wait_ge(s["res_made"], f)
                    act.dma_start(x_rows[:, :, :].rearrange("p (j t) f -> p j t f", j=2), x_pair[f])\
                        .then_inc(s["x_landed"], DMA)

                def square_x():
                    act.wait_ge(s["x_landed"], DMA * (f + 1))
                    squares(s, 2 * f, x_rows, sums[:, 2 * n:3 * n], range(n)).then_inc(s["squared"], 1)

                def lift_x(j):
                    act.wait_ge(s["x_turned"], 2 * f + j + 1)
                    wait(act, s["projected"], 2 * f + j)
                    a.activation(lifted[:, 1, :], ps_turn, ACT.Copy).then_inc(s["xT_made"], 1)

                def copy_products(j):
                    act.wait_ge(s["projected"], 2 * f + j + 1)
                    wait(act, s["res_made"], f)
                    a.activation(side[:, 4 * j:4 * j + 4, :].rearrange("p (k t) c -> p k t c", k=2), ps_x,
                                 ACT.Copy).then_inc(s["products_copied"], 1)

                return hooks_of(FRONT_ACT, (
                    ("load_x", load_x), ("square_x", square_x),
                    ("copy_0", lambda: lift_x(0)), ("products_0", lambda: copy_products(0)),
                    ("copy_1", lambda: lift_x(1)),
                    ("products_1", lambda: copy_products(1)), ("even", lambda: lift_block(2 * f, 0))))

            def back(f):
                s, N = pair_s, pair_numbers
                n = TILES

                def v_rooted():
                    act.wait_ge(s["v_clamped"], f + 1)
                    estimate_root(N, s, "v_rooted", PAIR_ROOTS * f, n)

                def v_tanh():
                    act.wait_ge(s["v_normed"], f + 1)
                    a.activation(N.th, N.norm[:, 0:n], ACT.Tanh).then_inc(s["v_tanh"], 1)

                def square_y():
                    for j in range(2):
                        act.wait_ge(s["y_made"], 2 * f + j + 1)
                        last = squares(s, 2 * f + 1, y_rows, N.sq[:, n:2 * n], range(4 * j, 4 * j + 4))
                    last.then_inc(s["squared"], 1)

                def rooted():
                    act.wait_ge(s["sq_clamped"], f + 1)
                    estimate_root(N, s, "sq_rooted", PAIR_ROOTS * f + 1, 2 * n)

                def scale_bias():
                    act.wait_ge(s["coefs_made"], f + 1)
                    for t in range(n):
                        last = a.activation(side[:, t, 0:D], b_layer[:, :], ACT.Copy, scale=N.c_b[:, t:t + 1])
                        if t % 4 == 3:
                            last.then_inc(s["bias_scaled"], 1)

                def var_rooted():
                    act.wait_ge(s["var_clamped"], f + 1)
                    estimate_root(N, s, "var_rooted", PAIR_ROOTS * f + 2, n)

                def store():
                    act.wait_ge(s["shift_made"], f + 1)
                    for t in range(n):
                        last = a.activation(y_rows[:, t, :], y_rows[:, t, :], ACT.Identity, bias=N.tmp[:, t:t + 1],
                                            scale=N.rsq[:, t:t + 1])
                    last.then_inc(s["out_made"], 1)
                    act.wait_ge(s["out_made"], f + 1)
                    act.dma_start(out_pair[f], y_rows[:, :, :].rearrange("p (j t) f -> p j t f", j=2))\
                        .then_inc(s["stored"], DMA)

                return hooks_of(BACK_ACT, (
                    ("odd", lambda: lift_block(2 * f + 1, 1)), ("v_rooted", v_rooted), ("v_tanh", v_tanh),
                    ("square_y", square_y), ("rooted", rooted),
                    ("log", lambda: take_log(N, s, "log_asked", "log_taken", f)),
                    ("tanh", lambda: take_tanh(N, s, f)), ("scale_bias", scale_bias), ("var_rooted", var_rooted),
                    ("store", store)))

            act.dma_start(w_embed[:, 0:D], embed).then_inc(consts_in, DMA)
            act.dma_start(b_embed[:, :], embed_bias.rearrange("(a n) -> a n", a=1).to_broadcast([P, D]))\
                .then_inc(consts_in, DMA)
            act.dma_start(b_layer[:, :], layer_bias.rearrange("(a n) -> a n", a=1).to_broadcast([P, D]))\
                .then_inc(consts_in, DMA)
            act.dma_start(w_x[:, 0:D], layer[0:P, :]).then_inc(consts_in, DMA)
            act.dma_start(w_v[:, 0:D], layer[P:2 * P, :]).then_inc(consts_in, DMA)
            first, second = number_stages(0), number_stages(1)
            for g in range(PERIOD):
                take_x(g)
                run(zip(L_ACT, first), g)
            bias_rows(0)
            bias_rows(1)
            high_L(0)
            L_hooks = list(zip(L_ACT_HOOKS, second))
            for w in range(PERIOD):
                if w + 2 < PERIOD:
                    L_hooks.append((w, lambda w=w: bias_rows(w + 2)))
                if w + 1 < PERIOD:
                    L_hooks.append((w, lambda w=w: high_L(w + 1)))
            schedule(nc.scalar, blocks, front, back, L_hooks)
            act.wait_ge(pair_s["stored"], DMA * PAIRS)

        @block.gpsimd
        def _(pool):
            g = nc.gpsimd
            g.memset(ident[:, :], 0.0).then_inc(ident_zero, 1)
            pool.wait_ge(ident_zero, 1)
            g.affine_select(out=ident[:, :], in_=ident[:, :], compare_op=ALU.not_equal, fill=1.0, base=0,
                            pattern=[[-1, P]], channel_multiplier=1).then_inc(consts_set, 1)

            def blocks(m, hooks):
                for j in range(2):
                    b = 2 * m + j
                    for w in range(PERIOD):
                        if KINDS[w] == "S" and PERIOD * j + w not in LOW_BY_VECTOR:
                            slot = place(j, w)[0]
                            for _, n, cols, high in halves_of(j, w):
                                pool.wait_ge(high_made, HALVES * 2 * len(SPLIT) * m + n + 1)
                                g.tensor_tensor(a_low[slot][:, :, cols], a_in[slot][:, :, cols],
                                                a_high[:, high].bitcast(F32), ALU.subtract)\
                                    .then_inc(low_by_pool, 1)
                        run(hooks, PERIOD * j + w)

            schedule(nc.gpsimd, blocks, nothing, nothing)

        @block.tensor
        def _(pe):
            t_e = nc.tensor

            def blocks(m, hooks):
                for j in range(2):
                    b = 2 * m + j
                    bank = acc[j].rearrange("p (g r) -> p g r", r=R)
                    for w in range(PERIOD):
                        if w == 0:
                            wait(pe, block_copied, b - 1)
                        at_start = isinstance(b, int) and b == 0
                        slot, at = place(j, w)
                        if KINDS[w] == "M":
                            if at_start:
                                pe.wait_ge(L_exact_made, w + 1)
                            pe.wait_ge(unit_turned, PERIOD * b + w + 1)
                            for i in range(UNIT_TILES):
                                last = t_e.matmul(bank, L_whole[:, UNIT_TILES * WHOLE.index(w) + i, :],
                                                  a_in[slot][:, :, at + R * i:at + R * (i + 1)],
                                                  start=False, stop=w == PERIOD - 1 and i == UNIT_TILES - 1)
                            last.then_inc(half_multiplied, HALVES)
                        else:
                            if at_start:
                                pe.wait_ge(L_low_made, ORDER[w] + 1)
                            for e, n, cols, high_slot in halves_of(j, w):
                                pe.wait_ge(*low_made(m, j, w, e))
                                for i in range(HALF):
                                    tile = UNIT_TILES * ORDER[w] + HALF * e + i
                                    low = a_low[slot][:, :, cols.start + R * i:cols.start + R * (i + 1)]
                                    high = a_high[:, high_slot, :, R * i:R * (i + 1)]
                                    first = w == 0 and e == 0 and i == 0
                                    end = w == PERIOD - 1 and e == HALVES - 1 and i == HALF - 1
                                    t_e.matmul(bank, L_high[:, tile, :], high, start=first, stop=False)
                                    t_e.matmul(bank, L_high[:, tile, :], low, start=False, stop=False)
                                    last = t_e.matmul(bank, L_low[:, tile, :], high, start=False, stop=end)
                                last.then_inc(half_multiplied, 1)
                        run(hooks, PERIOD * j + w)

            def project_all_x():
                s = L_s
                for g in range(PERIOD + 1):
                    if g < PERIOD:
                        if g % (PERIOD // X_PARTS) == 0:
                            pe.wait_ge(x_in[g // (PERIOD // X_PARTS)], QUADS * DMA)
                        wait(pe, s["xT_made"], g - 1)
                        for i in range(UNIT_TILES):
                            last = t_e.transpose(ps_turn_L[g % 2][:, P * i:P * (i + 1)],
                                                 x_all[:, UNIT_TILES * g + i, :], ident[:, :])
                        last.then_inc(s["x_turned"], 1)
                    if g > 0:
                        k = g - 1
                        pe.wait_ge(s["xT_made"], k + 1)
                        wait(pe, s["u_taken"], k - 1)
                        for i in range(UNIT_TILES):
                            last = t_e.matmul(ps_u[k % 2][:, i // 2, i % 2, :], lifted[:, k % 2, P * i:P * (i + 1)],
                                              w_embed[:, :], start=True, stop=True)
                        last.then_inc(s["projected"], 1)

            def turn_x(f, j):
                pe.wait_ge(pair_s["x_landed"], DMA * (f + 1))
                wait(pe, pair_s["xT_made"], 2 * f + j)
                for t in range(4):
                    last = t_e.transpose(ps_turn[:, P * t:P * (t + 1)], x_rows[:, 4 * j + t, :], ident[:, :])
                last.then_inc(pair_s["x_turned"], 1)

            def project_x(f, j):
                pe.wait_ge(pair_s["xT_made"], 2 * f + j + 1)
                wait(pe, pair_s["products_copied"], 2 * f + j)
                for t in range(4):
                    last = t_e.matmul(ps_x[:, t // 2, t % 2, :], lifted[:, 1, P * t:P * (t + 1)], w_x[:, :],
                                      start=True, stop=True)
                last.then_inc(pair_s["projected"], 1)

            def project_block(f, j):
                pe.wait_ge(block_copied, 2 * f + j + 1)
                wait(pe, pair_s["y_made"], 2 * f)
                wait(pe, pair_s["sums_taken"], f)
                vT = lifted[:, 0, :].rearrange("f (p t) -> f t p", t=4)
                squaresT = v_sqT[:, :].rearrange("f (p t) -> f t p", t=4)
                for t in range(4):
                    at = 4 * j + t
                    t_e.matmul(ps_v[at], vT[:, t, :], w_v[:, :], start=True, stop=True)
                    last = t_e.matmul(ps_v_sq[:, at:at + 1], squaresT[:, t, :], ones[:, :], start=True, stop=True)
                last.then_inc(block_projected, 1)

            def front(f):
                return hooks_of(FRONT_PE, (
                    ("turn_0", lambda: turn_x(f, 0)), ("project_0", lambda: project_x(f, 0)),
                    ("turn_1", lambda: turn_x(f, 1)), ("project_1", lambda: project_x(f, 1)),
                    ("even", lambda: project_block(f, 0))))

            def back(f):
                return hooks_of(BACK_PE, (("odd", lambda: project_block(f, 1)),))

            pe.wait_ge(consts_in, 5 * DMA)
            pe.wait_ge(consts_set, 2)
            pe.wait_ge(bias_done, 5)
            project_all_x()
            schedule(nc.tensor, blocks, front, back)


def kernel(x, adj, L0_gnn_embed, L0_gnn_layer, L0_gnn_embed_bias, L0_gnn_layer_bias):
    import numpy as np
    import concourse.bacc as bacc
    from concourse.bass_utils import run_bass_kernel_spmd

    nc = bacc.Bacc("TRN2", target_bir_lowering=False, num_devices=1)
    given = {"x": x, "adj": adj, "embed": L0_gnn_embed, "layer": L0_gnn_layer, "embed_bias": L0_gnn_embed_bias,
             "layer_bias": L0_gnn_layer_bias}
    arrays = {name: np.ascontiguousarray(a) for name, a in given.items()}
    drams = {name: nc.dram_tensor(name, a.shape, mybir.dt.from_np(a.dtype), kind="ExternalInput").ap()
             for name, a in arrays.items()}
    out = nc.dram_tensor("out", arrays["x"].shape, F32, kind="ExternalOutput").ap()
    graph_layer(nc, out=out, **drams)
    result = run_bass_kernel_spmd(nc, [arrays], core_ids=[0])
    return result.results[0]["out"]
```
